# Optimizing a Trainium2 kernel written in Bass

```python
import numpy as np
import jax
import jax.numpy as jnp

def _softmax(x, axis=-1):
    return jax.nn.softmax(x, axis=axis)
def _gelu(x):
    return jax.nn.gelu(x, approximate=True)
def _silu(x):
    return jax.nn.silu(x)
def _sigmoid(x):
    return jax.nn.sigmoid(x)
def _layernorm(x, axis=-1, eps=1e-5):
    m = jnp.mean(x, axis=axis, keepdims=True)
    v = jnp.var(x, axis=axis, keepdims=True)
    return (x - m) / jnp.sqrt(v + eps)
def _scatter_add(tgt, idx, src, axis=0):
    return tgt.at[idx].add(src)
def _segment_sum(src, seg, n):
    return jax.ops.segment_sum(src, seg, n)

kernel_name = 'mk_adj_resnorm_d1_adj_256_bd3f8d'

def setup_inputs(seed: int = 0):
    np.random.seed(seed)
    _w = jnp.asarray
    def _rec_inputs():
        import jax
        import jax.numpy as jnp
        _gk = jax.random.key(seed)
        x = -0.0005146 + 1 * jax.random.normal(jax.random.fold_in(_gk, 1), (8, 2048, 256), jnp.float32)
        _w = (1.0 + jnp.arange(2048, dtype=jnp.float32)) ** -0.5
        _w = _w / _w.mean()
        _pij = jnp.clip(0.00195312 * _w[:, None] * _w[None, :], 0.0, 1.0)
        _a = jax.random.uniform(jax.random.fold_in(_gk, 2), (8, 2048, 2048)) < _pij
        adj = _a.astype(jnp.int32)
        return x, adj
    x, adj = _rec_inputs()
    def _L0_gnn_setup():
        import jax, jax.numpy as jnp
        import numpy as np
        B, N, C, OUT, S = (4, 2048, 256, 256, 25)
        DENSITY = 0.008
        key = jax.random.key(seed)
        kA, kX, kW = jax.random.split(key, 3)
        A = jax.random.bernoulli(kA, DENSITY, (B, N, N)).astype(jnp.int32)
        X = jax.random.normal(kX, (B, N, C), dtype=jnp.float32)
        W = jax.random.normal(kW, (2 * C, OUT), dtype=jnp.float32) * np.float32(1.0 / np.sqrt(2 * C))
        b = jnp.zeros((OUT,), dtype=jnp.float32)
        return {'A': A, 'X': X, 'W': W, 'b': b}
    _L0_gnn_all = _L0_gnn_setup()
    _L0_gnn_in = {k: v for k, v in _L0_gnn_all.items() if k in ('W', 'b', )}
    del _L0_gnn_all

    return {
        "x": x,
        "adj": adj,
        "L0_gnn_W": _L0_gnn_in["W"],
        "L0_gnn_b": _L0_gnn_in["b"],
    }

def reference(x, adj, L0_gnn_W, L0_gnn_b):
    import jax
    import jax.numpy as jnp
    def _L0_gnn_ref(A, X, W, b):
        import jax, jax.numpy as jnp
        import numpy as np
        B, N, C, OUT, S = (4, 2048, 256, 256, 25)
        DENSITY = 0.008
        mask = A != 0
        neg_inf = jnp.float32(-jnp.inf)
        pri = -jnp.arange(N, dtype=jnp.float32)
        scores = jnp.where(mask, pri, neg_inf)
        vals, idx = jax.lax.top_k(scores, S)
        valid = vals > neg_inf
        feats = jax.vmap(lambda x, i: x[i])(X, idx)
        feats = jnp.where(valid[..., None], feats, neg_inf)
        agg = feats.max(axis=2)
        degree = mask.sum(axis=-1)
        agg = jnp.where((degree <= S)[..., None], jnp.maximum(agg, 0.0), agg)
        h = jnp.concatenate([X, agg], axis=-1)
        out = jax.nn.relu(jnp.einsum('bnf,fo->bno', h, W) + b)
        return out

    x = _layernorm(x + _L0_gnn_ref(adj, x, L0_gnn_W, L0_gnn_b), axis=-1)
    return x


_drawn_inputs = setup_inputs


def setup_inputs(seed=0):
    import zlib

    import numpy as np

    out = dict(_drawn_inputs(seed))
    spreads = {'L0_gnn_b': (0.0, 0.1)}
    factors = {}
    for name, (base, spread) in spreads.items():
        noise = np.random.default_rng([zlib.crc32(name.encode()), seed]).standard_normal(out[name].shape)
        drawn = base * np.exp(spread * noise) if base else spread * noise
        out[name] = jnp.asarray(drawn.astype(out[name].dtype))
    for name, factor in factors.items():
        out[name] = (out[name] * factor).astype(out[name].dtype)
    return out
```

```python
import concourse.bass as bass
from concourse import mybir
from contextlib import ExitStack

B, N, C, OUT, S = 8, 2048, 256, 256, 25
EPS = 1e-5
P = 128
TILES = B * N // P
U = 4
QUADS = TILES // U
QUADS_PER_BATCH = N // P // U
GROUP = 16
GROUPS = N // GROUP
TOP = 8
MAXROUNDS = -(-S // TOP)
FMAX = 3.4028234663852886e38

KEY_OPS = 2
ROUND_OPS = {1: 1 + 5 + 1, 2: 3 + 5 + 3, 4: 7 + 5 + 7}
EXTRACT_OPS = KEY_OPS + ROUND_OPS[4] + 3


def build(nc, x, adj, w, b, out):
    f32, bf16, i32 = mybir.dt.float32, mybir.dt.bfloat16, mybir.dt.int32
    ALU, ACT, AX = mybir.AluOpType, mybir.ActivationFunctionType, mybir.AxisListType

    x_rows = x.rearrange("b n c -> (b n) c")
    x_tiles = x.rearrange("b (t p) c -> (b t) p c", p=P)
    adj_tiles = adj.rearrange("b (t p) j -> (b t) p j", p=P)
    out_tiles = out.rearrange("b (t p) c -> (b t) p c", p=P)

    with ExitStack() as ctx:
        def sb(name, shape, dt=f32):
            return ctx.enter_context(nc.sbuf_tensor(name, shape, dt))

        def ps(name, shape, dt=f32):
            return ctx.enter_context(nc.psum_tensor(name, shape, dt))

        def sem(name):
            return ctx.enter_context(nc.semaphore(name))

        ident = sb("ident", [P, P])
        bit_diag = sb("bit_diag", [P, GROUP, P], bf16)
        ones_row = sb("ones_row", [1, P])
        bias_row = sb("bias_row", [1, OUT])
        weights = sb("weights", [P, 2 * C // P, OUT])
        eps_col = sb("eps_col", [P, 1])
        group_base = sb("group_base", [P, GROUPS])
        bit_mask = sb("bit_mask", [P, GROUP], i32)
        bit_score = sb("bit_score", [P, GROUP], i32)
        batch_base = sb("batch_base", [P, QUADS])
        adj_in = sb("adj_in", [P, U, N], i32)
        mask = sb("mask", [P, 2, N], bf16)
        mask_copy = sb("mask_copy", [P, N], bf16)
        degree = sb("degree", [P, U])
        dmax_raw = sb("dmax_raw", [1, U])
        dmax = sb("dmax", [1, U], i32)
        dmax_sum = sb("dmax_sum", [1, U], i32)
        cap = sb("cap", [P, U])
        floor = sb("floor", [P, U])
        key_lift = sb("key_lift", [P, GROUPS])
        keys = sb("keys", [P, 2, GROUPS])
        top_keys = sb("top_keys", [P, MAXROUNDS * TOP])
        top_int = sb("top_int", [P, MAXROUNDS * TOP], i32)
        top_group = sb("top_group", [P, MAXROUNDS * TOP], i32)
        bits = sb("bits", [P, MAXROUNDS * TOP, GROUP], i32)
        scores = sb("scores", [P, MAXROUNDS * TOP, GROUP])
        cand = sb("cand", [P, 2, MAXROUNDS * TOP * GROUP])
        found = sb("found", [P, MAXROUNDS * TOP])
        first = sb("first", [P, 1])
        pad = sb("pad", [P, MAXROUNDS * TOP])
        padded = sb("padded", [P, MAXROUNDS * TOP])
        index = [sb(f"index{u}", [P, MAXROUNDS * TOP], i32) for u in range(U)]
        gathered = [sb(f"gathered{u}", [P, S, C]) for u in range(U)]
        agg_raw = sb("agg_raw", [P, C])
        agg = sb("agg", [P, 2, C])
        x_in = sb("x_in", [P, U, C])
        h_t = sb("h_t", [P, 2, 2 * C // P, P])
        resid = sb("resid", [P, 2, OUT])
        stats = sb("stats", [P, 6])
        moments = sb("moments", [P, 2, 2])
        std = sb("std", [P, 2])
        rstd = sb("rstd", [P, 1])
        y = sb("y", [P, U, OUT])

        ps_words = [ps(f"ps_words{i}", [P, GROUPS]) for i in range(2)]
        ps_deg = ps("ps_deg", [1, P])
        ps_ht = [ps(f"ps_ht{i}", [P, 2 * C // P, P]) for i in range(2)]
        ps_out = [ps(f"ps_out{i}", [P, OUT]) for i in range(2)]

        const_loaded = sem("const_loaded")
        pool_const = sem("pool_const")
        const_ready = sem("const_ready")
        adj_loaded = [sem(f"adj_loaded{u}") for u in range(U)]
        x_loaded = [sem(f"x_loaded{u}") for u in range(U)]
        stored = [sem(f"stored{u}") for u in range(U)]
        gather_done = [sem(f"gather_done{u}") for u in range(U)]
        mask_ready = sem("mask_ready")
        words_ready = sem("words_ready")
        degree_ready = sem("degree_ready")
        degree_row_ready = sem("degree_row_ready")
        dmax_step = sem("dmax_step")
        dmax_ready = sem("dmax_ready")
        extract_step = sem("extract_step")
        index_ready = sem("index_ready")
        agg_raw_ready = sem("agg_raw_ready")
        agg_ready = sem("agg_ready")
        xt_ready = sem("xt_ready")
        ht_ready = sem("ht_ready")
        hw_ready = sem("hw_ready")
        resid_ready = sem("resid_ready")
        stats_ready = sem("stats_ready")
        moments_ready = sem("moments_ready")
        std_ready = sem("std_ready")
        rstd_ready = sem("rstd_ready")
        y_ready = sem("y_ready")
        held = sem("held")

        def hold(eng, semaphore, value):
            eng.wait_ge(semaphore, value)
            eng.sem_inc(held, 1)

        def quads(eng, steps):
            for u in range(U):
                steps(0, u)
            with eng.Fori(1, QUADS - 1) as q:
                for u in range(U):
                    steps(q, u)
            for u in range(U):
                steps(QUADS - 1, u)

        def tile(q, u, ahead):
            dq, v = divmod(u + ahead, U)
            qq = q + dq
            if isinstance(q, int) and not 0 <= qq < QUADS:
                return None
            return qq, v, qq * U + v

        block = ctx.enter_context(nc.Block())

        @block.sync
        def _(sp):
            sp.dma_start(weights[:, :, :], w.rearrange("(k p) o -> p k o", p=P)).then_inc(const_loaded, 16)
            sp.dma_start(bias_row[:, :], b.rearrange("(a o) -> a o", a=1)).then_inc(const_loaded, 16)

            def load_adj(qq, v, t):
                sp.dma_start(adj_in[:, v, :], adj_tiles[bass.ds(t, 1), :, :].rearrange("a p j -> (a p) j")).then_inc(adj_loaded[v], 16)

            def load_x(qq, v, t):
                sp.dma_start(x_in[:, v, :], x_tiles[bass.ds(t, 1), :, :].rearrange("a p j -> (a p) j")).then_inc(x_loaded[v], 16)

            def store(qq, v, t):
                sp.wait_ge(y_ready, t + 1)
                sp.dma_start(out_tiles[bass.ds(t, 1), :, :].rearrange("a p j -> (a p) j"), y[:, v, :]).then_inc(stored[v], 16)

            for u in range(U):
                load_adj(0, u, u)
                load_x(0, u, u)
            for u in range(U):
                sp.wait_ge(mask_ready, u + 1)
                load_adj(1, u, u + U)

            def steps(q, u):
                if t := tile(q, u, 2 * U):
                    sp.wait_ge(mask_ready, t[2] - U + 1)
                    load_adj(*t)
                if t := tile(q, u, 2):
                    if not isinstance(q, int) or t[2] >= U:
                        sp.wait_ge(resid_ready, t[2] - U + 1)
                        load_x(*t)
                if t := tile(q, u, -2):
                    store(*t)

            for u in range(U):
                steps(0, u)
            with sp.Fori(1, QUADS - 2) as q:
                for u in range(U):
                    steps(q, u)
            for q in (QUADS - 2, QUADS - 1):
                for u in range(U):
                    steps(q, u)
            for t in (TILES - 2, TILES - 1):
                store(QUADS - 1, t % U, t)
            for u in range(U):
                sp.wait_ge(stored[u], 16 * QUADS)

        @block.gpsimd
        def _(pool):
            nc.gpsimd.memset(ident[:, :], 0.0).then_inc(pool_const, 1)
            nc.gpsimd.memset(bit_diag[:, :, :], 0.0).then_inc(pool_const, 1)
            nc.gpsimd.memset(dmax_sum[:, :], 0).then_inc(const_ready, 1)
            nc.gpsimd.memset(ones_row[:, :], 1.0).then_inc(const_ready, 1)
            nc.gpsimd.memset(eps_col[:, :], EPS).then_inc(const_ready, 1)
            nc.gpsimd.iota(group_base[:, :], [[-1, GROUPS]], base=GROUPS - 1, channel_multiplier=0,
                           allow_small_or_imprecise_dtypes=True).then_inc(pool_const, 1)
            nc.gpsimd.iota(bit_score[:, :], [[-1, GROUP]], base=GROUP + 1, channel_multiplier=0).then_inc(const_ready, 1)
            for k in range(GROUP):
                nc.gpsimd.memset(bit_mask[:, k:k + 1], 2 ** (GROUP - 1 - k)).then_inc(const_ready, 1)
            nc.gpsimd.iota(batch_base[:, :], [[N, B], [0, QUADS_PER_BATCH]], base=N + 1, channel_multiplier=0,
                           allow_small_or_imprecise_dtypes=True).then_inc(const_ready, 1)
            pool.wait_ge(pool_const, 3)
            nc.gpsimd.tensor_scalar(group_base[:, :], group_base[:, :], 65536.0, 0.0, ALU.mult, ALU.add).then_inc(const_ready, 1)
            nc.gpsimd.affine_select(out=ident[:, :], in_=ident[:, :], compare_op=ALU.not_equal, fill=1.0,
                                    base=0, pattern=[[-1, P]], channel_multiplier=1).then_inc(const_ready, 1)
            for k in range(GROUP):
                nc.gpsimd.affine_select(out=bit_diag[:, k, :], in_=bit_diag[:, k, :], compare_op=ALU.not_equal,
                                        fill=float(2 ** (GROUP - 1 - k)), base=0, pattern=[[-1, P]],
                                        channel_multiplier=1).then_inc(const_ready, 1)

            def gather(u, slot):
                nc.gpsimd.indirect_dma_start(
                    gathered[u][:, slot, :], None, x_rows,
                    bass.IndirectOffsetOnAxis(ap=index[u][:, slot:slot + 1], axis=0),
                    bounds_check=B * N - 1, oob_is_err=False).then_inc(gather_done[u], 16)

            def gather_from(u, slot, most):
                if slot == S:
                    return
                with pool.If(most > slot):
                    gather(u, slot)
                    gather_from(u, slot + 1, most)

            def steps(q, u):
                t = q * U + u
                hold(pool, index_ready, t + 1)
                most = pool.value_load(dmax[0:1, u:u + 1], min_val=1, max_val=S)
                if not isinstance(q, int) or q > 0:
                    hold(pool, agg_raw_ready, t - U + 1)
                gather(u, 0)
                gather_from(u, 1, most)

            quads(pool, steps)

        NCONST = 5 + GROUP + 2 + GROUP

        @block.tensor
        def _(pe):
            pe.wait_ge(const_loaded, 32)
            pe.wait_ge(const_ready, NCONST)

            def pack(qq, v, t):
                pe.wait_ge(mask_ready, t + 1)
                if not isinstance(t, int) or t >= 2:
                    pe.wait_ge(extract_step, (t - 2) * EXTRACT_OPS + KEY_OPS)
                cols = mask[:, v % 2, :].rearrange("p (g k) -> p k g", k=GROUP)
                for k in range(GROUP):
                    last = nc.tensor.matmul(ps_words[v % 2][:, :], bit_diag[:, k, :], cols[:, k, :],
                                            start=(k == 0), stop=(k == GROUP - 1))
                last.then_inc(words_ready, 1)

            def degree_row(qq, v, t):
                pe.wait_ge(degree_ready, t + 1)
                if not isinstance(t, int) or t >= 1:
                    pe.wait_ge(dmax_ready, t)
                nc.tensor.transpose(ps_deg[:, :], degree[:, v:v + 1], ident[:, :]).then_inc(degree_row_ready, 1)

            def product(qq, v, t):
                pe.wait_ge(x_loaded[v], 16 * (qq + 1))
                pe.wait_ge(agg_ready, t + 1)
                if not isinstance(t, int) or t >= 2:
                    pe.wait_ge(ht_ready, t - 1)
                for k in range(2):
                    nc.tensor.transpose(ps_ht[v % 2][:, k, :], x_in[:, v, k * P:(k + 1) * P], ident[:, :])
                for k in range(2):
                    last = nc.tensor.transpose(ps_ht[v % 2][:, 2 + k, :], agg[:, v % 2, k * P:(k + 1) * P], ident[:, :])
                last.then_inc(xt_ready, 1)
                if not isinstance(t, int) or t >= 2:
                    pe.wait_ge(resid_ready, t - 1)
                nc.tensor.matmul(ps_out[v % 2][:, :], ones_row[:, :], bias_row[:, :], start=True, stop=False)
                pe.wait_ge(ht_ready, t + 1)
                for k in range(4):
                    last = nc.tensor.matmul(ps_out[v % 2][:, :], h_t[:, v % 2, k, :], weights[:, k, :],
                                            start=False, stop=(k == 3))
                last.then_inc(hw_ready, 1)

            for t in range(U):
                pack(0, t, t)
                if t < 3:
                    degree_row(0, t, t)

            def steps(q, u):
                if t := tile(q, u, 3):
                    degree_row(*t)
                if t := tile(q, u, 4):
                    pack(*t)
                if t := tile(q, u, -1):
                    product(*t)

            quads(pe, steps)
            product(QUADS - 1, U - 1, TILES - 1)

        @block.scalar
        def _(act):
            act.wait_ge(const_ready, NCONST)

            def count_degree(qq, v, t):
                act.wait_ge(mask_ready, t + 1)
                if not isinstance(t, int) or t >= 1:
                    act.wait_ge(degree_ready, t)
                if not isinstance(t, int) or t >= U:
                    act.wait_ge(index_ready, t - U + 1)
                nc.scalar.activation(mask_copy[:, :], mask[:, v % 2, :], ACT.Copy,
                                     accum_out=degree[:, v:v + 1]).then_inc(degree_ready, 1)

            def copy_ht(qq, v, t):
                act.wait_ge(xt_ready, t + 1)
                if not isinstance(t, int) or t >= 2:
                    act.wait_ge(hw_ready, t - 1)
                nc.scalar.activation(h_t[:, v % 2, :, :], ps_ht[v % 2][:, :, :], ACT.Copy).then_inc(ht_ready, 1)

            def root(qq, v, t):
                act.wait_ge(moments_ready, t + 1)
                if not isinstance(t, int) or t >= 2:
                    act.wait_ge(rstd_ready, t - 1)
                nc.scalar.activation(std[:, v % 2:v % 2 + 1], moments[:, v % 2, 1:2], ACT.Sqrt,
                                     bias=eps_col[:, :]).then_inc(std_ready, 1)

            for t in range(U):
                count_degree(0, t, t)

            def steps(q, u):
                if t := tile(q, u, -1):
                    copy_ht(*t)
                if t := tile(q, u, 4):
                    count_degree(*t)
                if t := tile(q, u, -2):
                    root(*t)

            quads(act, steps)
            copy_ht(QUADS - 1, U - 1, TILES - 1)
            root(QUADS - 1, U - 2, TILES - 2)
            root(QUADS - 1, U - 1, TILES - 1)

        @block.vector
        def _(dve):
            dve.wait_ge(const_ready, NCONST)

            def make_mask(qq, v, t):
                dve.wait_ge(adj_loaded[v], 16 * (qq + 1))
                if not isinstance(t, int) or t >= 2:
                    dve.wait_ge(words_ready, t - 1)
                    dve.wait_ge(degree_ready, t - 1)
                nc.vector.tensor_scalar(mask[:, v % 2, :], adj_in[:, v, :], 0.0, None, ALU.not_equal).then_inc(mask_ready, 1)

            def largest_degree(qq, v, t):
                dve.wait_ge(degree_row_ready, t + 1)
                nc.vector.tensor_reduce(dmax_raw[:, v:v + 1], ps_deg[:, :], AX.X, ALU.max).then_inc(dmax_step, 1)
                dve.wait_ge(dmax_step, 2 * t + 1)
                nc.vector.tensor_scalar(dmax[:, v:v + 1], dmax_raw[:, v:v + 1], float(S), 1.0, ALU.min, ALU.max).then_inc(dmax_step, 1)
                dve.wait_ge(dmax_step, 2 * t + 2)
                nc.vector.scalar_tensor_tensor(out=dmax_sum[:, v:v + 1], in0=dmax[:, v:v + 1], scalar=16.0, in1=dmax_sum[:, v:v + 1],
                                               op0=ALU.mult, op1=ALU.add).then_inc(dmax_ready, 1)

            def extract(qq, v, t):
                done = [0]

                def link(ins, alone=False):
                    done[0] += 1
                    ins.then_inc(extract_step, 1)
                    if alone:
                        hold(dve, extract_step, t * EXTRACT_OPS + done[0])
                    else:
                        dve.wait_ge(extract_step, t * EXTRACT_OPS + done[0])

                dve.wait_ge(words_ready, t + 1)
                hold(dve, dmax_ready, t + 1)
                most = dve.value_load(dmax[0:1, v:v + 1], min_val=1, max_val=S)
                nc.vector.tensor_scalar(cap[:, v:v + 1], degree[:, v:v + 1], 1.0, FMAX, ALU.min, ALU.mult)
                nc.vector.tensor_scalar(floor[:, v:v + 1], degree[:, v:v + 1], float(S), -FMAX, ALU.is_gt, ALU.mult)
                link(nc.vector.scalar_tensor_tensor(out=key_lift[:, :], in0=ps_words[v % 2][:, :], scalar=float(2 ** 23),
                                                    in1=group_base[:, :], op0=ALU.mult, op1=ALU.min))
                link(nc.vector.tensor_tensor(keys[:, 0, :], ps_words[v % 2][:, :], key_lift[:, :], ALU.add), alone=True)

                def top(values, where, rounds):
                    link(nc.vector.max(where[:, 0:TOP], values[:, 0, :]), alone=rounds > 1)
                    for r in range(1, rounds):
                        link(nc.vector.match_replace(values[:, r % 2, :], where[:, (r - 1) * TOP:r * TOP],
                                                     values[:, (r - 1) % 2, :], 0.0), alone=True)
                        link(nc.vector.max(where[:, r * TOP:(r + 1) * TOP], values[:, r % 2, :]), alone=r < rounds - 1)

                def expand(rounds):
                    n = rounds * TOP
                    start = done[0]
                    top(keys, top_keys, rounds)
                    link(nc.vector.tensor_copy(top_int[:, 0:n], top_keys[:, 0:n]))
                    nc.vector.tensor_scalar(top_group[:, 0:n], top_int[:, 0:n], 16, 4,
                                            ALU.logical_shift_right, ALU.logical_shift_left).then_inc(extract_step, 1)
                    done[0] += 1
                    link(nc.vector.tensor_tensor(bits[:, 0:n, :], top_int[:, 0:n].unsqueeze(2).to_broadcast([P, n, GROUP]),
                                                 bit_mask[:, :].unsqueeze(1).to_broadcast([P, n, GROUP]), ALU.bitwise_and))
                    nc.vector.tensor_tensor(scores[:, 0:n, :], top_group[:, 0:n].unsqueeze(2).to_broadcast([P, n, GROUP]),
                                            bit_score[:, :].unsqueeze(1).to_broadcast([P, n, GROUP]), ALU.add).then_inc(extract_step, 1)
                    done[0] += 1
                    dve.wait_ge(extract_step, t * EXTRACT_OPS + done[0])
                    link_cand(rounds, n)
                    assert done[0] - start == ROUND_OPS[rounds]
                    return start

                def link_cand(rounds, n):
                    view = cand[:, :, 0:n * GROUP]
                    link(nc.vector.scalar_tensor_tensor(out=view[:, 0, :], in0=bits[:, 0:n, :].rearrange("p n k -> p (n k)"), scalar=0.0,
                                                        in1=scores[:, 0:n, :].rearrange("p n k -> p (n k)"), op0=ALU.is_gt, op1=ALU.mult), alone=True)
                    top(view, found, rounds)

                def finish(rounds):
                    n = rounds * TOP
                    link(nc.vector.tensor_scalar(first[:, :], found[:, 0:1], 2.0, None, ALU.max))
                    link(nc.vector.tensor_scalar(pad[:, 0:n], found[:, 0:n], 0.0, first[:, :], ALU.is_equal, ALU.mult))
                    link(nc.vector.tensor_tensor(padded[:, 0:n], pad[:, 0:n], found[:, 0:n], ALU.add))
                    base = batch_base[:, qq:qq + 1] if isinstance(qq, int) else batch_base[:, bass.ds(qq, 1)]
                    nc.vector.tensor_scalar(index[v][:, 0:n], padded[:, 0:n], -1.0, base, ALU.mult, ALU.add).then_inc(index_ready, 1)

                def branch(rounds):
                    expand(rounds)
                    finish(rounds)
                    left = EXTRACT_OPS - done[0]
                    if left:
                        dve.sem_inc(extract_step, left)

                with dve.If(most > 2 * TOP):
                    branch(4)
                with dve.Else():
                    done[0] = KEY_OPS
                    with dve.If(most > TOP):
                        branch(2)
                    with dve.Else():
                        done[0] = KEY_OPS
                        branch(1)

            def maximum(qq, v, t):
                most = dve.value_load(dmax[0:1, v:v + 1], min_val=1, max_val=S)
                gathers = dve.value_load(dmax_sum[0:1, v:v + 1], min_val=16, max_val=16 * S * QUADS)
                hold(dve, gather_done[v], gathers)
                slots = gathered[v][:, :, :].rearrange("p s c -> p c s")

                def reduce_up_to(lo, hi):
                    if lo == hi:
                        nc.vector.tensor_reduce(agg_raw[:, :], slots[:, :, 0:lo], AX.X, ALU.max).then_inc(agg_raw_ready, 1)
                        return
                    mid = (lo + hi) // 2
                    with dve.If(most > mid):
                        reduce_up_to(mid + 1, hi)
                    with dve.Else():
                        reduce_up_to(lo, mid)

                reduce_up_to(1, S)
                dve.wait_ge(agg_raw_ready, t + 1)
                if not isinstance(t, int) or t >= 2:
                    dve.wait_ge(xt_ready, t - 1)
                nc.vector.tensor_scalar(agg[:, v % 2, :], agg_raw[:, :], cap[:, v:v + 1], floor[:, v:v + 1],
                                        ALU.min, ALU.max).then_inc(agg_ready, 1)

            def residual(qq, v, t):
                dve.wait_ge(hw_ready, t + 1)
                if not isinstance(t, int) or t >= 2:
                    dve.wait_ge(y_ready, t - 1)
                nc.vector.scalar_tensor_tensor(out=resid[:, v % 2, :], in0=ps_out[v % 2][:, :], scalar=0.0,
                                               in1=x_in[:, v, :], op0=ALU.max, op1=ALU.add).then_inc(resid_ready, 1)
                dve.wait_ge(resid_ready, t + 1)
                nc.vector.bn_stats(stats[:, :], resid[:, v % 2, :]).then_inc(stats_ready, 1)
                hold(dve, stats_ready, t + 1)
                nc.vector.bn_aggr(moments[:, v % 2, :], stats[:, :]).then_inc(moments_ready, 1)

            def normalise(qq, v, t):
                dve.wait_ge(std_ready, t + 1)
                nc.vector.reciprocal(rstd[:, :], std[:, v % 2:v % 2 + 1]).then_inc(rstd_ready, 1)
                dve.wait_ge(rstd_ready, t + 1)
                if not isinstance(t, int) or t >= U:
                    dve.wait_ge(stored[v], 16 * qq)
                nc.vector.tensor_scalar(y[:, v, :], resid[:, v % 2, :], moments[:, v % 2, 0:1], rstd[:, :],
                                        ALU.subtract, ALU.mult).then_inc(y_ready, 1)

            for t in range(2):
                make_mask(0, t, t)
            for t in range(2):
                largest_degree(0, t, t)
                extract(0, t, t)
            for t in range(2, U):
                make_mask(0, t, t)
            largest_degree(0, 2, 2)

            def steps(q, u):
                if t := tile(q, u, 4):
                    make_mask(*t)
                if t := tile(q, u, 3):
                    largest_degree(*t)
                if t := tile(q, u, 2):
                    extract(*t)
                if t := tile(q, u, -2):
                    normalise(*t)
                if t := tile(q, u, -1):
                    residual(*t)
                maximum(*tile(q, u, 0))

            quads(dve, steps)
            normalise(QUADS - 1, U - 2, TILES - 2)
            residual(QUADS - 1, U - 1, TILES - 1)
            normalise(QUADS - 1, U - 1, TILES - 1)


_INS = ['x', 'adj', 'L0_gnn_W', 'L0_gnn_b']
_OUTS = [((8, 2048, 256), 'float32')]


def kernel(**inputs):
    import numpy as _np
    import concourse.bacc as _bacc
    from concourse import mybir as _mybir
    from concourse.bass_utils import run_bass_kernel_spmd as _run

    nc = _bacc.Bacc("TRN2", target_bir_lowering=False, num_devices=1)
    arrays, args = {}, []
    for name in _INS:
        a = _np.ascontiguousarray(inputs[name])
        arrays[f"in_{name}_dram"] = a
        args.append(nc.dram_tensor(f"in_{name}_dram", a.shape, _mybir.dt.from_np(a.dtype), kind="ExternalInput").ap())
    for i, (shape, dtype) in enumerate(_OUTS):
        dt = _mybir.dt.from_np(_np.dtype(dtype))
        args.append(nc.dram_tensor(f"out_{i}_dram", shape, dt, kind="ExternalOutput").ap())
    build(nc, *args)
    r = _run(nc, [arrays], core_ids=[0])
    return r.results[0]["out_0_dram"]
```
